# Optimizing a Trainium2 kernel written in Bass

```python
import numpy as np
import jax
import jax.numpy as jnp

def _softmax(x, axis=-1):
    return jax.nn.softmax(x, axis=axis)

def _gelu(x):
    return jax.nn.gelu(x, approximate=True)

def _silu(x):
    return jax.nn.silu(x)

def _sigmoid(x):
    return jax.nn.sigmoid(x)

def _layernorm(x, axis=-1, eps=1e-05):
    m = jnp.mean(x, axis=axis, keepdims=True)
    v = jnp.var(x, axis=axis, keepdims=True)
    return (x - m) / jnp.sqrt(v + eps)

def _scatter_add(tgt, idx, src, axis=0):
    return tgt.at[idx].add(src)

def _segment_sum(src, seg, n):
    return jax.ops.segment_sum(src, seg, n)
kernel_name = 'mk_adaln_ffn_d1_seqx_r4_d0a503'

def setup_inputs(seed: int=0):
    np.random.seed(seed)
    _w = jnp.asarray

    def _rec_inputs():
        import jax
        import jax.numpy as jnp
        _rk = jax.random.key(seed)
        x = -0.000125 + 0.9999 * jax.random.normal(jax.random.fold_in(_rk, 1), (32, 64, 1024), jnp.float32)
        _lenS = 64 - jax.random.randint(jax.random.fold_in(_rk, 7), (32,), 0, max(1, 64 // 4) + 1, jnp.int32)
        _lenS2 = 64 - jax.random.randint(jax.random.fold_in(_rk, 8), (32,), 0, max(1, 64 // 4) + 1, jnp.int32)
        cond_128 = 0.0061147 + 1.02565 * jax.random.normal(jax.random.fold_in(_rk, 11), (32, 128), jnp.float32)
        return (x, cond_128)
    x, cond_128 = _rec_inputs()

    def _L0_cond_setup():
        import jax, jax.numpy as jnp
        import numpy as np
        K = 8
        T = 1.0
        D_EMBD = 128
        IN_C = 64
        OUT_C = 64
        BS = 32
        H = 1024
        HID = 128
        key = jax.random.key(seed)
        ks = jax.random.split(key, 10)
        s = lambda fan_in: 1.0 / np.sqrt(fan_in)
        return {'x': jax.random.normal(ks[0], (BS, IN_C, H), dtype=jnp.float32), 'embedding': jax.random.normal(ks[1], (BS, D_EMBD), dtype=jnp.float32), 'W0': jax.random.normal(ks[2], (D_EMBD, HID), dtype=jnp.float32) * s(D_EMBD), 'b0': jnp.zeros((HID,), dtype=jnp.float32), 'W1': jax.random.normal(ks[3], (HID, HID), dtype=jnp.float32) * s(HID), 'b1': jnp.zeros((HID,), dtype=jnp.float32), 'W2': jax.random.normal(ks[4], (HID, K), dtype=jnp.float32) * s(HID), 'b2': jnp.zeros((K,), dtype=jnp.float32), 'weight': jax.random.normal(ks[5], (K, OUT_C, IN_C, 1), dtype=jnp.float32) * s(IN_C), 'bias_k': jax.random.normal(ks[6], (K, OUT_C), dtype=jnp.float32) * 0.1}
    _L0_cond_all = _L0_cond_setup()
    _L0_cond_in = {k: v for k, v in _L0_cond_all.items() if k in ('W0', 'b0', 'W1', 'b1', 'W2', 'b2', 'weight', 'bias_k')}
    del _L0_cond_all

    def _L0_ffn_setup():
        import jax, jax.numpy as jnp
        import numpy as np
        B, L, H, Dh, M = (4, 512, 16, 64, 256)
        D = H * Dh
        key = jax.random.key(seed)
        kx, ku, kd, kp = jax.random.split(key, 4)
        x = jax.random.normal(kx, (B, L, D), dtype=jnp.float32)
        up = jax.random.normal(ku, (H, Dh, M), dtype=jnp.float32)
        down = jax.random.normal(kd, (H, M, Dh), dtype=jnp.float32)
        perm = jax.random.permutation(kp, D)
        return {'x': x, 'up': up, 'down': down, 'perm': perm}
    _L0_ffn_all = _L0_ffn_setup()
    _L0_ffn_in = {k: v for k, v in _L0_ffn_all.items() if k in ('up', 'down', 'perm')}
    del _L0_ffn_all
    return {'x': x, 'cond_128': cond_128, 'L0_cond_W0': _L0_cond_in['W0'], 'L0_cond_b0': _L0_cond_in['b0'], 'L0_cond_W1': _L0_cond_in['W1'], 'L0_cond_b1': _L0_cond_in['b1'], 'L0_cond_W2': _L0_cond_in['W2'], 'L0_cond_b2': _L0_cond_in['b2'], 'L0_cond_weight': _L0_cond_in['weight'], 'L0_cond_bias_k': _L0_cond_in['bias_k'], 'L0_ffn_up': _L0_ffn_in['up'], 'L0_ffn_down': _L0_ffn_in['down'], 'L0_ffn_perm': _L0_ffn_in['perm']}

def reference(x, cond_128, L0_cond_W0, L0_cond_b0, L0_cond_W1, L0_cond_b1, L0_cond_W2, L0_cond_b2, L0_cond_weight, L0_cond_bias_k, L0_ffn_up, L0_ffn_down, L0_ffn_perm):
    import jax
    import jax.numpy as jnp

    def _L0_cond_ref(x, embedding, W0, b0, W1, b1, W2, b2, weight, bias_k):
        import jax, jax.numpy as jnp
        import numpy as np
        K = 8
        T = 1.0
        D_EMBD = 128
        IN_C = 64
        OUT_C = 64
        BS = 32
        H = 1024
        HID = 128
        h = jax.nn.gelu(embedding @ W0 + b0, approximate=False)
        h = jax.nn.gelu(h @ W1 + b1, approximate=False)
        att = jax.nn.softmax((h @ W2 + b2) / T, axis=-1)
        agg_w = jnp.einsum('bk,koi->boi', att, weight[..., 0])
        agg_b = att @ bias_k
        out = jnp.einsum('boi,bih->boh', agg_w, x) + agg_b[:, :, None]
        return out

    def _L0_ffn_ref(x, up, down, perm):
        import jax, jax.numpy as jnp
        import numpy as np
        B, L, H, Dh, M = (4, 512, 16, 64, 256)
        D = H * Dh
        b, l, Dm = x.shape
        h, d = (up.shape[0], up.shape[1])
        unperm = jnp.argsort(perm)
        t = x.reshape(b * l, Dm)
        t = t[:, perm]
        t = t.reshape(b * l, h, d)
        t = jnp.einsum('bhd,hdm->bhm', t, up)
        t = jax.nn.gelu(t, approximate=False)
        t = jnp.einsum('bhm,hmd->bhd', t, down)
        t = t.reshape(b * l, h * d)
        t = t[:, unperm]
        out = t.reshape(b, l, Dm)
        return out
    x = x + _L0_ffn_ref(_L0_cond_ref(x, cond_128, L0_cond_W0, L0_cond_b0, L0_cond_W1, L0_cond_b1, L0_cond_W2, L0_cond_b2, L0_cond_weight, L0_cond_bias_k), L0_ffn_up, L0_ffn_down, L0_ffn_perm)
    return x

_drawn_inputs = setup_inputs


def setup_inputs(seed=0):
    import zlib

    import numpy as np

    out = dict(_drawn_inputs(seed))
    spreads = {'L0_cond_b0': (0.0, 0.1), 'L0_cond_b1': (0.0, 0.1), 'L0_cond_b2': (0.0, 0.1)}
    factors = {}
    for name, (base, spread) in spreads.items():
        noise = np.random.default_rng([zlib.crc32(name.encode()), seed]).standard_normal(out[name].shape)
        drawn = base * np.exp(spread * noise) if base else spread * noise
        out[name] = jnp.asarray(drawn.astype(out[name].dtype))
    for name, factor in factors.items():
        out[name] = (out[name] * factor).astype(out[name].dtype)
    return out
```

```python
import concourse.bass as bass
from concourse import mybir
from contextlib import ExitStack

B, CH, D = 32, 64, 1024
H, DH, M = 16, 64, 256
E_IN, HID, K = 128, 128, 8
P = 128
TOK = B * CH
TW = 512
QT = TOK // TW
CHUNKS = D // P
TILES = CHUNKS * QT
PAIRS = TW // P
HEADS = P // DH
MC = M // P
RING = 2 * QT
LAG = 2
OB = CH // 16
ROWS = D * QT

C_EMB = 0
C_W0 = C_EMB + B
C_W1 = C_W0 + HID
C_W2 = C_W1 + HID
C_B0 = C_W2 + K
C_B1 = C_B0 + 1
C_B2 = C_B1 + 1
C_ID = C_B2 + K
C_SEL = C_ID + P
C_COND = C_SEL + 16
C_BK = C_COND
C_WK = C_BK + OB
C_ALL = C_WK + OB * P


def adaln_ffn(nc, xt, perm, packed, up_l, down_l, out):
    f32, f32r, i32 = mybir.dt.float32, mybir.dt.float32r, mybir.dt.int32
    ALU, ACT, AX = mybir.AluOpType, mybir.ActivationFunctionType, mybir.AxisListType

    ctx = ExitStack()
    with ctx:
        def sb(name, shape, dt=f32):
            return ctx.enter_context(nc.sbuf_tensor(name, shape, dt))

        def sem(name):
            return ctx.enter_context(nc.semaphore(name))

        cond = sb("cond", [P, C_ALL])
        h1 = sb("h1", [P, B])
        h2 = sb("h2", [P, B])
        logits = sb("logits", [B, K])
        top = sb("top", [B, 1])
        neg_top = sb("neg_top", [B, 1])
        expd = sb("expd", [B, K])
        total = sb("total", [B, 1])
        inv_total = sb("inv_total", [B, 1])
        att_rep = sb("att_rep", [B, K, 16])
        att_sel = sb("att_sel", [P, B, 16])
        bias_lhs = sb("bias_lhs", [P, OB, P])
        mix_w = sb("mix_w", [P, B // 2, 2, CH])
        mix_b = sb("mix_b", [P, B, CH])
        perm_sb = sb("perm_sb", [P, CHUNKS], i32)
        idx_all = sb("idx_all", [P, CHUNKS, QT], i32)
        idx = sb("idx", [P, RING], i32)
        g = sb("g", [P, RING, TW])
        xp = sb("xp", [P, 2, TW])
        t = sb("t", [P, 2, TW])
        ts = sb("ts", [P, 2, HEADS, TW], f32r)
        hid = sb("hid", [P, 2, MC, HEADS, TW])
        up_raw = sb("up_raw", [P, 2, HEADS, M])
        up_hi = sb("up_hi", [P, 2, HEADS, M], f32r)
        up_lo = sb("up_lo", [P, 2, HEADS, M], f32r)
        dn = sb("dn", [P, 2, HEADS, MC, DH])

        ps = ctx.enter_context(nc.psum_tensor("ps", [P, 8, TW], f32))
        HB, XB, TB, YB = 0, 4, 5, 6

        s_perm, s_cond, s_experts = sem("s_perm"), sem("s_cond"), sem("s_experts")
        s_idx_all, s_idx, s_passed = sem("s_idx_all"), sem("s_idx"), sem("s_passed")
        s_zero = sem("s_zero")
        s_cmm, s_cact, s_cdve = sem("s_cmm"), sem("s_cact"), sem("s_cdve")
        s_aggw, s_aggb, s_mixw, s_mixb = sem("s_aggw"), sem("s_aggb"), sem("s_mixw"), sem("s_mixb")
        s_gathered = [sem(f"s_gathered{r}") for r in range(RING)]
        s_scattered = [sem(f"s_scattered{r}") for r in range(RING)]
        s_up = [sem(f"s_up{r}") for r in range(2)]
        s_dn = [sem(f"s_dn{r}") for r in range(2)]
        s_up_hi, s_up_split = sem("s_up_hi"), sem("s_up_split")
        s_trans, s_xp = sem("s_trans"), sem("s_xp")
        s_mix, s_t = sem("s_mix"), sem("s_t")
        s_hi, s_lo = sem("s_hi"), sem("s_lo")
        s_upped, s_gelu = sem("s_upped"), sem("s_gelu")
        s_down, s_final = sem("s_down"), sem("s_final")

        def steps(eng, step):
            for r in range(-3, 1):
                step(0, r)
            with eng.Fori(0, TILES - 2 * RING + 1, RING) as base:
                for r in range(1, RING + 1):
                    step(base, r)
            for r in range(1, RING):
                step(TILES - RING, r)

        def exists(base, r):
            return not isinstance(base, int) or 0 <= base + r < TILES

        block = ctx.enter_context(nc.Block())

        @block.sync
        def _(sp):
            sp.dma_start(perm_sb[:, :], perm).then_inc(s_perm, 16)
            sp.dma_start(cond[:, 0:C_COND], packed[:, 0:C_COND]).then_inc(s_cond, 16)

            def load(up_row, down_row, r):
                for half in range(2):
                    sp.dma_start(up_raw[half * DH:(half + 1) * DH, r, :, :].rearrange("p e m -> p (e m)"),
                                 up_l[bass.ds(up_row, DH), :]).then_inc(s_up[r], 16)
                sp.dma_start(dn[:, r, :, :, :].rearrange("p e c d -> p (e c d)"),
                             down_l[bass.ds(down_row, P), :]).then_inc(s_dn[r], 16)

            sp.dma_start(cond[:, C_COND:C_ALL], packed[:, C_COND:C_ALL]).then_inc(s_experts, 16)
            for r in range(2):
                load(r * DH, r * P, r)
            with sp.Fori(2, CHUNKS - 1, 2) as chunk:
                for r in range(2):
                    sp.wait_ge(s_down, (chunk + (r - 1)) * QT)
                    load((chunk + r) * DH, (chunk + r) * P, r)

        @block.gpsimd
        def _(pool):
            nc.gpsimd.memset(mix_w[:, :, :, :], 0.0).then_inc(s_zero, 1)
            pool.wait_ge(s_idx_all, QT)
            nc.gpsimd.tensor_copy(idx[:, :], idx_all[:, 0:2, :].rearrange("p c q -> p (c q)")).then_inc(s_idx, 1)
            pool.wait_ge(s_idx, 1)

            def gather(r):
                pool.indirect_dma_start(out=g[:, r, :], out_offset=None, in_=xt,
                                        in_offset=bass.IndirectOffsetOnAxis(ap=idx[:, r:r + 1], axis=0),
                                        ).then_inc(s_gathered[r], 16)

            def split(base, c):
                r = c % 2
                pool.wait_ge(s_up[r], (base + c - r) * 16 + 32)
                if not isinstance(base, int) or base + c >= 2:
                    pool.wait_ge(s_upped, (base + (c - 1)) * QT * MC)
                    pool.sem_inc(s_passed, 1)
                nc.gpsimd.tensor_copy(up_hi[:, r, :, :], up_raw[:, r, :, :]).then_inc(s_up_hi, 1)
                pool.wait_ge(s_up_hi, base + c + 1)
                nc.gpsimd.tensor_tensor(up_lo[:, r, :, :], up_raw[:, r, :, :], up_hi[:, r, :, :].bitcast(f32),
                                        ALU.subtract).then_inc(s_up_split, 1)

            for r in range(RING):
                gather(r)
            split(0, 0)
            split(0, 1)

            def scatter(base, r):
                slot = r % RING
                pool.wait_ge(s_final, base + r + 1)
                pool.sem_inc(s_passed, 1)
                pool.indirect_dma_start(out=out,
                                        out_offset=bass.IndirectOffsetOnAxis(ap=idx[:, slot:slot + 1], axis=0),
                                        in_=g[:, slot, :], in_offset=None).then_inc(s_scattered[slot], 16)

            def refill(base, r):
                pool.wait_ge(s_scattered[r], base * (16 // RING) + 16)
                nc.gpsimd.tensor_copy(idx[:, r:r + 1], idx_flat[:, bass.ds(base + (RING + r), 1)]).then_inc(s_idx, 1)
                pool.wait_ge(s_idx, base + (r + 2))
                pool.sem_inc(s_passed, 1)
                gather(r)

            idx_flat = idx_all[:, :, :].rearrange("p c q -> p (c q)")
            for r in range(LAG):
                scatter(0, r)
            with pool.Fori(0, TILES - 2 * RING + 1, RING) as base:
                for r in range(RING):
                    scatter(base, r + LAG)
                    refill(base, r)
                    if r % QT == 1:
                        split(base // QT, 2 + r // QT)
            for r in range(LAG, RING):
                scatter(TILES - RING, r)
            for r in range(RING):
                pool.wait_ge(s_scattered[r], (TILES // RING) * 16)

        @block.scalar
        def _(act):
            b0, b1 = cond[:, C_B0:C_B0 + 1], cond[:, C_B1:C_B1 + 1]
            act.wait_ge(s_cmm, 1)
            nc.scalar.activation(h1[:, :], ps[:, YB, 0:B], ACT.Gelu, bias=b0).then_inc(s_cact, 1)
            act.wait_ge(s_cmm, 2)
            nc.scalar.activation(h2[:, :], ps[:, YB, 64:64 + B], ACT.Gelu, bias=b1).then_inc(s_cact, 1)
            act.wait_ge(s_cdve, 2)
            nc.scalar.activation(expd[:, :], logits[:, :], ACT.Exp, bias=neg_top[:, :],
                                 accum_out=total[:, :]).then_inc(s_cact, 1)
            act.wait_ge(s_zero, 1)
            act.wait_ge(s_aggw, 1)
            nc.scalar.activation(mix_w[DH:P, :, 1, :].rearrange("p a (n o) -> p n a o", n=OB),
                                 ps[DH:P, 0:OB, :].rearrange("p n (a h o) -> p n a h o", h=2, o=16)[:, :, :, 1, :],
                                 ACT.Copy).then_inc(s_mixw, 1)
            act.wait_ge(s_aggb, 1)
            nc.scalar.activation(mix_b[:, :, CH // 2:CH].rearrange("p b (n o) -> p n b o", o=16),
                                 ps[:, OB // 2:OB, :].rearrange("p n (b o) -> p n b o", o=16),
                                 ACT.Copy).then_inc(s_mixb, 1)

            def hi(base, r, e):
                if not exists(base, r):
                    return
                act.wait_ge(s_t, base + r + 1)
                if not isinstance(base, int) or base + r >= 2:
                    act.wait_ge(s_upped, (base + (r - 1)) * MC)
                rows = slice(e * DH, (e + 1) * DH)
                nc.scalar.activation(ts[rows, r % 2, e, :], t[rows, r % 2, :], ACT.Copy).then_inc(s_hi, 1)

            def gelu(base, r, c):
                if not exists(base, r):
                    return
                act.wait_ge(s_upped, (base + r) * MC + c + 1)
                if not isinstance(base, int) or base + r >= 2:
                    act.wait_ge(s_down, (base + (r - 1)))
                nc.scalar.activation(hid[:, r % 2, c, :, :], ps[:, HB + 2 * c:HB + 2 * c + 2, :],
                                     ACT.Gelu).then_inc(s_gelu, 1)

            def step(base, r):
                hi(base, r + 2, 1)
                gelu(base, r + 1, 1)
                hi(base, r + 3, 0)
                gelu(base, r + 2, 0)

            steps(act, step)

        @block.vector
        def _(dve):
            dve.wait_ge(s_perm, 16)
            for q in range(QT):
                nc.vector.tensor_scalar(idx_all[:, :, q], perm_sb[:, :], QT, q, ALU.mult, ALU.add).then_inc(s_idx_all, 1)
            dve.wait_ge(s_cmm, 3)
            nc.vector.tensor_tensor(logits[:, :], ps[0:B, YB, 128:128 + K], cond[0:B, C_B2:C_B2 + K],
                                    ALU.add).then_inc(s_cdve, 1)
            dve.wait_ge(s_cdve, 1)
            nc.vector.tensor_reduce(neg_top[:, :], logits[:, :], AX.X, ALU.max, negate=True).then_inc(s_cdve, 1)
            dve.wait_ge(s_cact, 3)
            nc.vector.reciprocal(inv_total[:, :], total[:, :]).then_inc(s_cdve, 1)
            dve.wait_ge(s_cdve, 3)
            nc.vector.tensor_scalar(att_rep[:, :, :], expd[:, :].rearrange("p (k a) -> p k a", a=1).broadcast_to((B, K, 16)),
                                    inv_total[:, :], None, ALU.mult).then_inc(s_cdve, 1)
            dve.wait_ge(s_experts, 16)
            nc.vector.tensor_copy(bias_lhs[:, :, :],
                                  cond[:, C_BK:C_BK + OB].rearrange("p (n a) -> p n a", a=1).broadcast_to((P, OB, P))).then_inc(s_cdve, 1)
            dve.wait_ge(s_cmm, 4)
            nc.vector.tensor_tensor(att_sel[:, :, :],
                                    ps[:, YB, 192:192 + B].rearrange("p (b a) -> p b a", a=1).broadcast_to((P, B, 16)),
                                    cond[:, C_SEL:C_SEL + 16].rearrange("p (a o) -> p a o", a=1).broadcast_to((P, B, 16)),
                                    ALU.mult).then_inc(s_cdve, 1)
            dve.wait_ge(s_zero, 1)
            dve.wait_ge(s_aggw, 1)
            nc.vector.tensor_copy(mix_w[0:DH, :, 0, :].rearrange("p a (n o) -> p n a o", n=OB),
                                  ps[0:DH, 0:OB, :].rearrange("p n (a h o) -> p n a h o", h=2, o=16)[:, :, :, 0, :]
                                  ).then_inc(s_mixw, 1)
            dve.wait_ge(s_aggb, 1)
            nc.vector.tensor_copy(mix_b[:, :, 0:CH // 2].rearrange("p b (n o) -> p n b o", o=16),
                                  ps[:, 0:OB // 2, :].rearrange("p n (b o) -> p n b o", o=16)
                                  ).then_inc(s_mixb, 1)

            def take_xp(base, r):
                if not exists(base, r):
                    return
                dve.wait_ge(s_trans, base + r + 1)
                if not isinstance(base, int) or base + r >= 2:
                    dve.wait_ge(s_mix, base + (r - 1))
                nc.vector.tensor_copy(xp[:, r % 2, :], ps[:, XB, :]).then_inc(s_xp, 1)

            def take_t(base, r):
                if not exists(base, r):
                    return
                q = r % QT
                if isinstance(base, int) and base + r == 0:
                    dve.wait_ge(s_mixb, 2)
                dve.wait_ge(s_mix, base + r + 1)
                if not isinstance(base, int) or base + r >= 2:
                    dve.wait_ge(s_hi, (base + (r - 1)) * HEADS)
                bq = B // QT
                nc.vector.tensor_tensor(t[:, r % 2, :], ps[:, TB, :],
                                        mix_b[:, q * bq:(q + 1) * bq, :].rearrange("p b o -> p (b o)"),
                                        ALU.add).then_inc(s_t, 1)

            def lo(base, r, e):
                if not exists(base, r):
                    return
                dve.wait_ge(s_hi, (base + r) * HEADS + e + 1)
                rows = slice(e * DH, (e + 1) * DH)
                other = slice((1 - e) * DH, (2 - e) * DH)
                nc.vector.tensor_tensor(ts[other, r % 2, e, :], t[rows, r % 2, :], ts[rows, r % 2, e, :].bitcast(f32),
                                        ALU.subtract).then_inc(s_lo, 1)

            def final(base, r):
                if not exists(base, r):
                    return
                dve.wait_ge(s_down, base + r + 1)
                nc.vector.tensor_tensor(g[:, r % RING, :], ps[:, YB + r % 2, :], g[:, r % RING, :],
                                        ALU.add).then_inc(s_final, 1)

            def step(base, r):
                final(base, r)
                take_xp(base, r + 3)
                lo(base, r + 2, 1)
                take_t(base, r + 3)
                lo(base, r + 3, 0)

            steps(dve, step)

        @block.tensor
        def _(pe):
            ident = cond[:, C_ID:C_ID + P]
            pe.wait_ge(s_cond, 16)
            nc.tensor.matmul(ps[:, YB, 0:B], cond[:, C_W0:C_W0 + HID], cond[:, C_EMB:C_EMB + B],
                             start=True, stop=True).then_inc(s_cmm, 1)
            pe.wait_ge(s_cact, 1)
            nc.tensor.matmul(ps[:, YB, 64:64 + B], cond[:, C_W1:C_W1 + HID], h1[:, :],
                             start=True, stop=True).then_inc(s_cmm, 1)
            pe.wait_ge(s_cact, 2)
            nc.tensor.matmul(ps[0:B, YB, 128:128 + K], h2[:, :], cond[:, C_W2:C_W2 + K],
                             start=True, stop=True).then_inc(s_cmm, 1)
            pe.wait_ge(s_cdve, 4)
            nc.tensor.matmul(ps[:, YB, 192:192 + B], att_rep[:, :, :].rearrange("p k a -> p (k a)"),
                             cond[0:B, C_ID:C_ID + B], start=True, stop=True).then_inc(s_cmm, 1)
            pe.wait_ge(s_experts, 16)
            pe.wait_ge(s_cdve, 6)
            rhs = att_sel[:, :, :].rearrange("p b o -> p (b o)")
            for n in range(OB):
                last = nc.tensor.matmul(ps[:, n, :], cond[:, C_WK + n * P:C_WK + (n + 1) * P], rhs,
                                        start=True, stop=True)
            last.then_inc(s_aggw, 1)
            pe.wait_ge(s_mixw, 2)
            for n in range(OB):
                last = nc.tensor.matmul(ps[:, n, :], bias_lhs[:, n, :], rhs, start=True, stop=True)
            last.then_inc(s_aggb, 1)

            def trans(base, r):
                if not exists(base, r):
                    return
                slot = r % RING
                pe.wait_ge(s_gathered[slot], (base + (r - slot)) * (16 // RING) + 16)
                if not isinstance(base, int) or base + r >= 1:
                    pe.wait_ge(s_xp, base + r)
                for a in range(PAIRS):
                    last = nc.tensor.transpose(ps[:, XB, a * P:(a + 1) * P], g[:, slot, a * P:(a + 1) * P], ident)
                last.then_inc(s_trans, 1)

            def mix(base, r):
                if not exists(base, r):
                    return
                pe.wait_ge(s_xp, base + r + 1)
                if not isinstance(base, int) or base + r >= 1:
                    pe.wait_ge(s_t, base + r)
                for a in range(PAIRS):
                    pair = (r % QT) * PAIRS + a
                    last = nc.tensor.matmul(ps[:, TB, a * P:(a + 1) * P], xp[:, r % 2, a * P:(a + 1) * P],
                                            mix_w[:, pair, :, :].rearrange("p h o -> p (h o)"),
                                            start=True, stop=True)
                last.then_inc(s_mix, 1)

            def up(base, r, c):
                if not exists(base, r):
                    return
                w = (r % RING) // QT
                if c == 0:
                    pe.wait_ge(s_lo, (base + r + 1) * HEADS)
                    if r % QT == 0:
                        pe.wait_ge(s_up_split, (base // QT) + (r // QT + 1))
                if not isinstance(base, int) or base + r >= 1:
                    pe.wait_ge(s_gelu, (base + (r - 1)) * MC + c + 1)
                for e in range(HEADS):
                    for n, wt in enumerate((up_hi, up_lo)):
                        last = nc.tensor.matmul(ps[:, HB + 2 * c + e, :], wt[:, w, e, c * P:(c + 1) * P],
                                                ts[:, r % 2, e, :], start=(n == 0), stop=(n == 1))
                last.then_inc(s_upped, 1)

            def down(base, r, c):
                if not exists(base, r):
                    return
                slot = r % RING
                w = slot // QT
                if c == 0:
                    if r % QT == 0:
                        pe.wait_ge(s_dn[w], (base + (r - slot)) * (16 // RING) + 16)
                    if not isinstance(base, int) or base + r >= 2:
                        pe.wait_ge(s_final, base + (r - 1))
                pe.wait_ge(s_gelu, (base + r) * MC + c + 1)
                for e in range(HEADS):
                    last = nc.tensor.matmul(ps[e * DH:(e + 1) * DH, YB + r % 2, :], dn[:, w, e, c, :],
                                            hid[:, r % 2, c, e, :], start=(c == 0), stop=(c == MC - 1))
                if c == MC - 1:
                    last.then_inc(s_down, 1)

            def step(base, r):
                down(base, r, 1)
                trans(base, r + 3)
                up(base, r + 1, 1)
                down(base, r + 1, 0)
                if exists(base, r + 3) and isinstance(base, int) and base + r + 3 == 0:
                    pe.wait_ge(s_mixw, 2)
                mix(base, r + 3)
                if exists(base, r + 2) and isinstance(base, int) and base + r + 2 == 0:
                    pe.wait_ge(s_mixb, 2)
                up(base, r + 2, 0)

            steps(pe, step)


def kernel(**inputs):
    import numpy as np
    import concourse.bacc as bacc
    from concourse import mybir as mb
    from concourse.bass_utils import run_bass_kernel_spmd

    a = {name: np.asarray(v) for name, v in inputs.items()}
    xt = np.ascontiguousarray(a["x"].reshape(TOK, D).T).reshape(ROWS, TW)
    perm = np.ascontiguousarray(a["L0_ffn_perm"].reshape(CHUNKS, P).T)
    bcast = lambda v: np.broadcast_to(v, (P,) + v.shape)
    experts = a["L0_cond_weight"].reshape(K, OB, 16, CH).transpose(0, 2, 1, 3).reshape(P, OB, 1, CH)
    bias_k = a["L0_cond_bias_k"].reshape(K, OB, 16).transpose(0, 2, 1).reshape(P, OB)
    packed = np.concatenate([
        a["cond_128"].T, a["L0_cond_W0"], a["L0_cond_W1"], a["L0_cond_W2"],
        a["L0_cond_b0"].reshape(P, 1), a["L0_cond_b1"].reshape(P, 1), bcast(a["L0_cond_b2"]),
        np.eye(P, dtype=np.float32), np.tile(np.eye(16, dtype=np.float32), (K, 1)),
        bias_k, np.broadcast_to(experts, (P, OB, 2, CH)).reshape(P, OB * P),
    ], axis=1)
    up_l = np.ascontiguousarray(a["L0_ffn_up"].reshape(CHUNKS, HEADS, DH, M).transpose(0, 2, 1, 3)).reshape(CHUNKS * DH, HEADS * M)
    down_l = np.ascontiguousarray(a["L0_ffn_down"].reshape(CHUNKS, HEADS, MC, P, DH).transpose(0, 3, 1, 2, 4)).reshape(CHUNKS * P, HEADS * MC * DH)

    nc = bacc.Bacc("TRN2", target_bir_lowering=False, num_devices=1)
    arrays, args = {}, []
    for name, v in (("xt", xt), ("perm", perm), ("packed", packed), ("up_l", up_l), ("down_l", down_l)):
        arrays[name] = v
        args.append(nc.dram_tensor(name, v.shape, mb.dt.from_np(v.dtype), kind="ExternalInput").ap())
    out = nc.dram_tensor("out", (ROWS, TW), mb.dt.float32, kind="ExternalOutput").ap()
    adaln_ffn(nc, *args, out)
    r = run_bass_kernel_spmd(nc, [arrays], core_ids=[0])
    got = r.results[0]["out"]
    return np.ascontiguousarray(got.reshape(D, TOK).T).reshape(B, CH, D)
```

```python
import concourse.bass as bass
from concourse import mybir
from contextlib import ExitStack

B, CH, D = 32, 64, 1024
H, DH, M = 16, 64, 256
E_IN, HID, K = 128, 128, 8
P = 128
TOK = B * CH
TW = 512
QT = TOK // TW
CHUNKS = D // P
TILES = CHUNKS * QT
BQ = B // QT
PAIRS = BQ // 2
HEADS = P // DH
MC = M // P
RING = 2 * QT
LAG = 2
OB = CH // 16
ROWS = D * QT

C_EMB = 0
C_W0 = C_EMB + B
C_B0 = C_W0 + HID
C_FIRST = C_B0 + 1
C_W1 = C_FIRST
C_B1 = C_W1 + HID
C_W2 = C_B1 + 1
C_B2 = C_W2 + K
C_ID = C_B2 + K
C_SEL = C_ID + P
C_BK = C_SEL + 16
C_COND = C_BK + CH
C_WK = C_COND
C_ALL = C_WK + OB * P


def adaln_ffn(nc, xt, perm, packed, up_l, down_l, out):
    f32, f32r, i32 = mybir.dt.float32, mybir.dt.float32r, mybir.dt.int32
    ALU, ACT, AX = mybir.AluOpType, mybir.ActivationFunctionType, mybir.AxisListType

    ctx = ExitStack()
    with ctx:
        def sb(name, shape, dt=f32):
            return ctx.enter_context(nc.sbuf_tensor(name, shape, dt))

        def sem(name):
            return ctx.enter_context(nc.semaphore(name))

        cond = sb("cond", [P, C_ALL])
        h1 = sb("h1", [P, B])
        h2 = sb("h2", [P, B])
        logits = sb("logits", [B, K])
        top = sb("top", [B, 1])
        neg_top = sb("neg_top", [B, 1])
        expd = sb("expd", [B, K])
        warm = sb("warm", [B, 1])
        total = sb("total", [B, 1])
        inv_total = sb("inv_total", [B, 1])
        att_rep = sb("att_rep", [B, K, 16])
        att_sel = sb("att_sel", [P, B, 16])
        att_t = sb("att_t", [P, B])
        mix_b_row = sb("mix_b_row", [B, CH])
        mix_w = sb("mix_w", [P, B // 2, 2, CH])
        mix_b = sb("mix_b", [P, TOK])
        bias_dram = nc.dram_tensor("bias_dram", (TOK,), f32, kind="Internal").ap()
        perm_sb = sb("perm_sb", [P, CHUNKS], i32)
        idx_all = sb("idx_all", [P, CHUNKS, QT], i32)
        idx = sb("idx", [P, RING], i32)
        g = sb("g", [P, RING, TW])
        xp = sb("xp", [P, 2, TW])
        t = sb("t", [P, 2, TW])
        ts = sb("ts", [P, 2, HEADS, TW], f32r)
        hid = sb("hid", [P, 2, MC, HEADS, TW])
        up_raw = sb("up_raw", [P, 2, HEADS, M])
        up_hi = sb("up_hi", [P, 2, HEADS, M], f32r)
        up_lo = sb("up_lo", [P, 2, HEADS, M], f32r)
        dn = sb("dn", [P, 2, HEADS, MC, DH])

        ps = ctx.enter_context(nc.psum_tensor("ps", [P, 8, TW], f32))
        HB, XB, TB, YB = 0, 4, 5, 6

        s_perm, s_first, s_cond, s_experts = sem("s_perm"), sem("s_first"), sem("s_cond"), sem("s_experts")
        s_idx_all, s_idx, s_passed = sem("s_idx_all"), sem("s_idx"), sem("s_passed")
        s_zero = sem("s_zero")
        s_cmm, s_cact, s_cdve = sem("s_cmm"), sem("s_cact"), sem("s_cdve")
        s_sel = sem("s_sel")
        s_att_t, s_aggb, s_bias_row, s_bias_out = sem("s_att_t"), sem("s_aggb"), sem("s_bias_row"), sem("s_bias_out")
        s_aggw, s_mixw_odd, s_mixw_even = sem("s_aggw"), sem("s_mixw_odd"), sem("s_mixw_even")
        s_mixb = [sem(f"s_mixb{q}") for q in range(QT)]
        s_gathered = [sem(f"s_gathered{r}") for r in range(RING)]
        s_scattered = [sem(f"s_scattered{r}") for r in range(RING)]
        s_up = [sem(f"s_up{r}") for r in range(2)]
        s_dn = [sem(f"s_dn{r}") for r in range(2)]
        s_up_hi, s_up_split = sem("s_up_hi"), sem("s_up_split")
        s_trans, s_xp = sem("s_trans"), sem("s_xp")
        s_mix, s_t = sem("s_mix"), sem("s_t")
        s_hi, s_lo = sem("s_hi"), sem("s_lo")
        s_upped, s_gelu = sem("s_upped"), sem("s_gelu")
        s_down, s_final = sem("s_down"), sem("s_final")

        def steps(eng, step):
            for r in range(-2, 3):
                step(0, r)
            with eng.Fori(0, TILES - 2 * RING + 1, RING) as base:
                for r in range(3, RING + 3):
                    step(base, r)
            for r in range(3, RING + 1):
                step(TILES - RING, r)

        def exists(base, r):
            return not isinstance(base, int) or 0 <= base + r < TILES

        def first(base, r):
            return r if isinstance(base, int) and base == 0 else None

        AB = [YB + 1, HB + 1, HB + 2, HB + 3]
        agg_w = [ps[:, bank, :].rearrange("p (n a h o) -> p n a h o", n=OB, h=2, o=16) for bank in AB]

        block = ctx.enter_context(nc.Block())

        @block.sync
        def _(sp):
            sp.dma_start(perm_sb[:, :], perm).then_inc(s_perm, 16)
            sp.dma_start(cond[:, C_FIRST:C_COND], packed[:, C_FIRST:C_COND]).then_inc(s_cond, 16)

            def load(up_row, down_row, r):
                for half in range(2):
                    sp.dma_start(up_raw[half * DH:(half + 1) * DH, r, :, :].rearrange("p e m -> p (e m)"),
                                 up_l[bass.ds(up_row, DH), :]).then_inc(s_up[r], 16)
                sp.dma_start(dn[:, r, :, :, :].rearrange("p e c d -> p (e c d)"),
                             down_l[bass.ds(down_row, P), :]).then_inc(s_dn[r], 16)

            sp.dma_start(cond[:, C_COND:C_ALL], packed[:, C_COND:C_ALL]).then_inc(s_experts, 16)
            load(0, 0, 0)
            sp.wait_ge(s_bias_row, 1)
            sp.dma_start(bias_dram.rearrange("(b o) -> b o", o=CH), mix_b_row[:, :]).then_inc(s_bias_out, 16)
            sp.wait_ge(s_bias_out, 16)
            for q in range(QT):
                sp.dma_start(mix_b[:, q * TW:(q + 1) * TW],
                             bias_dram[q * TW:(q + 1) * TW].rearrange("(a n) -> a n", a=1).broadcast_to((P, TW))
                             ).then_inc(s_mixb[q], 16)
            load(DH, P, 1)
            with sp.Fori(2, CHUNKS - 1, 2) as chunk:
                for r in range(2):
                    sp.wait_ge(s_down, (chunk + (r - 1)) * QT)
                    load((chunk + r) * DH, (chunk + r) * P, r)

        @block.gpsimd
        def _(pool):
            nc.gpsimd.memset(mix_w[:, :, :, :], 0.0).then_inc(s_zero, 1)
            pool.wait_ge(s_idx_all, QT)
            nc.gpsimd.tensor_copy(idx[:, :], idx_all[:, 0:2, :].rearrange("p c q -> p (c q)")).then_inc(s_idx, 1)
            pool.wait_ge(s_idx, 1)

            def gather(r):
                pool.indirect_dma_start(out=g[:, r, :], out_offset=None, in_=xt,
                                        in_offset=bass.IndirectOffsetOnAxis(ap=idx[:, r:r + 1], axis=0),
                                        ).then_inc(s_gathered[r], 16)

            def split(base, c):
                r = c % 2
                pool.wait_ge(s_up[r], (base + c - r) * 16 + 32)
                if not isinstance(base, int) or base + c >= 2:
                    pool.wait_ge(s_upped, (base + (c - 1)) * QT * MC)
                    pool.sem_inc(s_passed, 1)
                nc.gpsimd.tensor_copy(up_hi[:, r, :, :], up_raw[:, r, :, :]).then_inc(s_up_hi, 1)
                pool.wait_ge(s_up_hi, base + c + 1)
                nc.gpsimd.tensor_tensor(up_lo[:, r, :, :], up_raw[:, r, :, :], up_hi[:, r, :, :].bitcast(f32),
                                        ALU.subtract).then_inc(s_up_split, 1)

            for r in range(RING):
                gather(r)
                if r == 3:
                    split(0, 0)
            split(0, 1)

            def scatter(base, r):
                slot = r % RING
                pool.wait_ge(s_final, base + r + 1)
                pool.sem_inc(s_passed, 1)
                pool.indirect_dma_start(out=out,
                                        out_offset=bass.IndirectOffsetOnAxis(ap=idx[:, slot:slot + 1], axis=0),
                                        in_=g[:, slot, :], in_offset=None).then_inc(s_scattered[slot], 16)

            def refill(base, r):
                pool.wait_ge(s_scattered[r], base * (16 // RING) + 16)
                nc.gpsimd.tensor_copy(idx[:, r:r + 1], idx_flat[:, bass.ds(base + (RING + r), 1)]).then_inc(s_idx, 1)
                pool.wait_ge(s_idx, base + (r + 2))
                pool.sem_inc(s_passed, 1)
                gather(r)

            idx_flat = idx_all[:, :, :].rearrange("p c q -> p (c q)")
            for r in range(LAG):
                scatter(0, r)
            with pool.Fori(0, TILES - 2 * RING + 1, RING) as base:
                for r in range(RING):
                    scatter(base, r + LAG)
                    refill(base, r)
                    if r % QT == 2:
                        split(base // QT, 2 + r // QT)
            for r in range(LAG, RING):
                scatter(TILES - RING, r)
            for r in range(RING):
                pool.wait_ge(s_scattered[r], (TILES // RING) * 16)

        @block.scalar
        def _(act):
            b0, b1 = cond[:, C_B0:C_B0 + 1], cond[:, C_B1:C_B1 + 1]
            act.dma_start(cond[:, 0:C_FIRST], packed[:, 0:C_FIRST]).then_inc(s_first, 16)
            act.wait_ge(s_cmm, 1)
            nc.scalar.activation(h1[:, :], ps[:, HB, 0:B], ACT.Gelu, bias=b0).then_inc(s_cact, 1)
            act.wait_ge(s_cmm, 2)
            nc.scalar.activation(h2[:, :], ps[:, HB, 64:64 + B], ACT.Gelu, bias=b1).then_inc(s_cact, 1)
            act.wait_ge(s_cdve, 2)
            nc.scalar.activation(expd[:, :], logits[:, :], ACT.Exp, bias=neg_top[:, :],
                                 accum_out=total[:, :]).then_inc(s_cact, 1)
            nc.scalar.activation(warm[:, :], neg_top[:, :], ACT.Gelu)

            act.wait_ge(s_aggb, 1)
            nc.scalar.activation(mix_b_row[:, :], ps[0:B, YB, 0:CH], ACT.Copy).then_inc(s_bias_row, 1)

            def take_mix(q):
                if q == 0:
                    act.wait_ge(s_zero, 1)
                act.wait_ge(s_aggw, q + 1)
                nc.scalar.activation(mix_w[DH:P, q * PAIRS:(q + 1) * PAIRS, 1, :].rearrange("p a (n o) -> p n a o", n=OB),
                                     agg_w[q][DH:P, :, :, 1, :], ACT.Copy).then_inc(s_mixw_odd, 1)

            def hi(base, r, e):
                if not exists(base, r):
                    return
                act.wait_ge(s_t, base + r + 1)
                if not isinstance(base, int) or base + r >= 2:
                    act.wait_ge(s_upped, (base + (r - 1)) * MC)
                rows = slice(e * DH, (e + 1) * DH)
                nc.scalar.activation(ts[rows, r % 2, e, :], t[rows, r % 2, :], ACT.Copy).then_inc(s_hi, 1)

            def gelu(base, r, c):
                if not exists(base, r):
                    return
                act.wait_ge(s_upped, (base + r) * MC + c + 1)
                if not isinstance(base, int) or base + r >= 2:
                    act.wait_ge(s_down, (base + (r - 1)))
                nc.scalar.activation(hid[:, r % 2, c, :, :], ps[:, HB + 2 * c:HB + 2 * c + 2, :],
                                     ACT.Gelu).then_inc(s_gelu, 1)

            def step(base, r):
                if first(base, r) == -1:
                    for q in range(QT):
                        take_mix(q)
                hi(base, r + 1, 0)
                hi(base, r + 1, 1)
                gelu(base, r, 0)
                gelu(base, r, 1)

            steps(act, step)

        @block.vector
        def _(dve):
            dve.wait_ge(s_perm, 16)
            for q in range(QT):
                nc.vector.tensor_scalar(idx_all[:, :, q], perm_sb[:, :], QT, q, ALU.mult, ALU.add).then_inc(s_idx_all, 1)
            dve.wait_ge(s_cmm, 3)
            nc.vector.tensor_tensor(logits[:, :], ps[0:B, HB, 128:128 + K], cond[0:B, C_B2:C_B2 + K],
                                    ALU.add).then_inc(s_cdve, 1)
            dve.wait_ge(s_cdve, 1)
            nc.vector.tensor_reduce(neg_top[:, :], logits[:, :], AX.X, ALU.max, negate=True).then_inc(s_cdve, 1)
            dve.wait_ge(s_cact, 3)
            nc.vector.reciprocal(inv_total[:, :], total[:, :]).then_inc(s_cdve, 1)
            dve.wait_ge(s_cdve, 3)
            nc.vector.tensor_scalar(att_rep[:, :, :], expd[:, :].rearrange("p (k a) -> p k a", a=1).broadcast_to((B, K, 16)),
                                    inv_total[:, :], None, ALU.mult).then_inc(s_cdve, 1)
            dve.wait_ge(s_cmm, 4)

            def select(q):
                nc.vector.tensor_tensor(att_sel[:, q * BQ:(q + 1) * BQ, :],
                                        ps[:, HB, 192 + q * BQ:192 + (q + 1) * BQ].rearrange("p (b a) -> p b a", a=1).broadcast_to((P, BQ, 16)),
                                        cond[:, C_SEL:C_SEL + 16].rearrange("p (a o) -> p a o", a=1).broadcast_to((P, BQ, 16)),
                                        ALU.mult).then_inc(s_sel, 1)

            def take_mix(q):
                if q == 0:
                    dve.wait_ge(s_zero, 1)
                dve.wait_ge(s_aggw, q + 1)
                nc.vector.tensor_copy(mix_w[0:DH, q * PAIRS:(q + 1) * PAIRS, 0, :].rearrange("p a (n o) -> p n a o", n=OB),
                                      agg_w[q][0:DH, :, :, 0, :]).then_inc(s_mixw_even, 1)

            def take_xp(base, r):
                if not exists(base, r):
                    return
                dve.wait_ge(s_trans, base + r + 1)
                if not isinstance(base, int) or base + r >= 2:
                    dve.wait_ge(s_mix, base + (r - 1))
                nc.vector.tensor_copy(xp[:, r % 2, :], ps[:, XB, :]).then_inc(s_xp, 1)

            def take_t(base, r):
                if not exists(base, r):
                    return
                q = r % QT
                if isinstance(base, int) and base + r < QT:
                    dve.wait_ge(s_mixb[r], 16)
                dve.wait_ge(s_mix, base + r + 1)
                if not isinstance(base, int) or base + r >= 2:
                    dve.wait_ge(s_hi, (base + (r - 1)) * HEADS)
                nc.vector.tensor_tensor(t[:, r % 2, :], ps[:, TB, :],
                                        mix_b[:, q * TW:(q + 1) * TW],
                                        ALU.add).then_inc(s_t, 1)

            def lo(base, r, e):
                if not exists(base, r):
                    return
                dve.wait_ge(s_hi, (base + r) * HEADS + e + 1)
                rows = slice(e * DH, (e + 1) * DH)
                other = slice((1 - e) * DH, (2 - e) * DH)
                nc.vector.tensor_tensor(ts[other, r % 2, e, :], t[rows, r % 2, :], ts[rows, r % 2, e, :].bitcast(f32),
                                        ALU.subtract).then_inc(s_lo, 1)

            def final(base, r):
                if not exists(base, r):
                    return
                dve.wait_ge(s_down, base + r + 1)
                nc.vector.tensor_tensor(g[:, r % RING, :], ps[:, YB + r % 2, :], g[:, r % RING, :],
                                        ALU.add).then_inc(s_final, 1)

            nc.vector.tensor_copy(att_t[:, :], ps[:, HB, 192:192 + B]).then_inc(s_att_t, 1)
            select(0)

            def step(base, r):
                if first(base, r) == -1:
                    take_mix(0)
                    take_xp(base, r + 2)
                    take_mix(1)
                    take_mix(2)
                take_t(base, r + 1)
                if first(base, r) == -1:
                    take_mix(3)
                else:
                    take_xp(base, r + 2)
                lo(base, r + 1, 0)
                lo(base, r + 1, 1)
                if first(base, r) == -2:
                    for q in range(1, QT):
                        select(q)
                final(base, r - 1)

            steps(dve, step)

        @block.tensor
        def _(pe):
            ident = cond[:, C_ID:C_ID + P]
            pe.wait_ge(s_first, 16)

            def warm_up(n):
                for _ in range(n):
                    nc.tensor.matmul(ps[:, YB + 1, 0:HID], cond[:, C_W0:C_W0 + HID], cond[:, C_W0:C_W0 + HID],
                                     start=True, stop=True)

            nc.tensor.matmul(ps[:, HB, 0:B], cond[:, C_W0:C_W0 + HID], cond[:, C_EMB:C_EMB + B],
                             start=True, stop=True).then_inc(s_cmm, 1)
            warm_up(2)
            pe.wait_ge(s_cond, 16)
            pe.wait_ge(s_cact, 1)
            nc.tensor.matmul(ps[:, HB, 64:64 + B], cond[:, C_W1:C_W1 + HID], h1[:, :],
                             start=True, stop=True).then_inc(s_cmm, 1)
            warm_up(1)
            pe.wait_ge(s_cact, 2)
            nc.tensor.matmul(ps[0:B, HB, 128:128 + K], h2[:, :], cond[:, C_W2:C_W2 + K],
                             start=True, stop=True).then_inc(s_cmm, 1)
            def aggregate(q):
                if q == 0:
                    pe.wait_ge(s_experts, 16)
                pe.wait_ge(s_sel, q + 1)
                rhs = att_sel[:, q * BQ:(q + 1) * BQ, :].rearrange("p b o -> p (b o)")
                for n in range(OB):
                    last = nc.tensor.matmul(ps[:, AB[q], n * P:(n + 1) * P], cond[:, C_WK + n * P:C_WK + (n + 1) * P],
                                            rhs, start=True, stop=True)
                last.then_inc(s_aggw, 1)

            def trans(base, r):
                if not exists(base, r):
                    return
                slot = r % RING
                pe.wait_ge(s_gathered[slot], (base + (r - slot)) * (16 // RING) + 16)
                if not isinstance(base, int) or base + r >= 1:
                    pe.wait_ge(s_xp, base + r)
                for a in range(PAIRS):
                    last = nc.tensor.transpose(ps[:, XB, a * P:(a + 1) * P], g[:, slot, a * P:(a + 1) * P], ident)
                last.then_inc(s_trans, 1)

            warm_up(3)
            trans(0, 0)
            pe.wait_ge(s_cdve, 4)
            nc.tensor.matmul(ps[:, HB, 192:192 + B], att_rep[:, :, :].rearrange("p k a -> p (k a)"),
                             cond[0:B, C_ID:C_ID + B], start=True, stop=True).then_inc(s_cmm, 1)
            pe.wait_ge(s_att_t, 1)
            nc.tensor.matmul(ps[0:B, YB, 0:CH], att_t[:, :], cond[:, C_BK:C_BK + CH],
                             start=True, stop=True).then_inc(s_aggb, 1)

            warm_up(1)

            def mix(base, r):
                if not exists(base, r):
                    return
                pe.wait_ge(s_xp, base + r + 1)
                if isinstance(base, int) and base + r < QT:
                    pe.wait_ge(s_mixw_even, r + 1)
                    pe.wait_ge(s_mixw_odd, r + 1)
                if not isinstance(base, int) or base + r >= 1:
                    pe.wait_ge(s_t, base + r)
                for a in range(PAIRS):
                    pair = (r % QT) * PAIRS + a
                    last = nc.tensor.matmul(ps[:, TB, a * P:(a + 1) * P], xp[:, r % 2, a * P:(a + 1) * P],
                                            mix_w[:, pair, :, :].rearrange("p h o -> p (h o)"),
                                            start=True, stop=True)
                last.then_inc(s_mix, 1)

            def up(base, r, c):
                if not exists(base, r):
                    return
                w = (r % RING) // QT
                if c == 0:
                    if r % QT == 0:
                        pe.wait_ge(s_up_split, (base // QT) + (r // QT + 1))
                if not isinstance(base, int) or base + r >= 1:
                    pe.wait_ge(s_gelu, (base + (r - 1)) * MC + c + 1)
                else:
                    pe.wait_ge(s_mixw_even, QT)
                    pe.wait_ge(s_mixw_odd, QT)
                for e in range(HEADS):
                    if c == 0:
                        pe.wait_ge(s_lo, (base + r) * HEADS + (e + 1))
                    for n, wt in enumerate((up_hi, up_lo)):
                        last = nc.tensor.matmul(ps[:, HB + 2 * c + e, :], wt[:, w, e, c * P:(c + 1) * P],
                                                ts[:, r % 2, e, :], start=(n == 0), stop=(n == 1))
                last.then_inc(s_upped, 1)

            def down(base, r, c):
                if not exists(base, r):
                    return
                slot = r % RING
                w = slot // QT
                if c == 0:
                    if r % QT == 0:
                        pe.wait_ge(s_dn[w], (base + (r - slot)) * (16 // RING) + 16)
                    if not isinstance(base, int) or base + r >= 2:
                        pe.wait_ge(s_final, base + (r - 1))
                    elif base + r == 0:
                        pe.wait_ge(s_bias_row, 1)
                pe.wait_ge(s_gelu, (base + r) * MC + c + 1)
                for e in range(HEADS):
                    last = nc.tensor.matmul(ps[e * DH:(e + 1) * DH, YB + r % 2, :], dn[:, w, e, c, :],
                                            hid[:, r % 2, c, e, :], start=(c == 0), stop=(c == MC - 1))
                if c == MC - 1:
                    last.then_inc(s_down, 1)

            def step(base, r):
                if first(base, r) == -1:
                    aggregate(0)
                    aggregate(1)
                mix(base, r + 1)
                if first(base, r) != -2:
                    trans(base, r + 2)
                up(base, r, 0)
                up(base, r, 1)
                if first(base, r) == -1:
                    aggregate(2)
                    aggregate(3)
                down(base, r - 1, 0)
                down(base, r - 1, 1)

            steps(pe, step)


def kernel(**inputs):
    import numpy as np
    import concourse.bacc as bacc
    from concourse import mybir as mb
    from concourse.bass_utils import run_bass_kernel_spmd

    a = {name: np.asarray(v) for name, v in inputs.items()}
    xt = np.ascontiguousarray(a["x"].reshape(TOK, D).T).reshape(ROWS, TW)
    perm = np.ascontiguousarray(a["L0_ffn_perm"].reshape(CHUNKS, P).T)
    bcast = lambda v: np.broadcast_to(v, (P,) + v.shape)
    experts = a["L0_cond_weight"].reshape(K, OB, 16, CH).transpose(0, 2, 1, 3).reshape(P, OB, 1, CH)
    bias_k = np.zeros((K, 16, CH), np.float32)
    bias_k[:, 0] = a["L0_cond_bias_k"]
    packed = np.concatenate([
        a["cond_128"].T, a["L0_cond_W0"], a["L0_cond_b0"].reshape(P, 1),
        a["L0_cond_W1"], a["L0_cond_b1"].reshape(P, 1), a["L0_cond_W2"], bcast(a["L0_cond_b2"]),
        np.eye(P, dtype=np.float32), np.tile(np.eye(16, dtype=np.float32), (K, 1)),
        bias_k.reshape(P, CH), np.broadcast_to(experts, (P, OB, 2, CH)).reshape(P, OB * P),
    ], axis=1)
    up_l = np.ascontiguousarray(a["L0_ffn_up"].reshape(CHUNKS, HEADS, DH, M).transpose(0, 2, 1, 3)).reshape(CHUNKS * DH, HEADS * M)
    down_l = np.ascontiguousarray(a["L0_ffn_down"].reshape(CHUNKS, HEADS, MC, P, DH).transpose(0, 3, 1, 2, 4)).reshape(CHUNKS * P, HEADS * MC * DH)

    nc = bacc.Bacc("TRN2", target_bir_lowering=False, num_devices=1)
    arrays, args = {}, []
    for name, v in (("xt", xt), ("perm", perm), ("packed", packed), ("up_l", up_l), ("down_l", down_l)):
        arrays[name] = v
        args.append(nc.dram_tensor(name, v.shape, mb.dt.from_np(v.dtype), kind="ExternalInput").ap())
    out = nc.dram_tensor("out", (ROWS, TW), mb.dt.float32, kind="ExternalOutput").ap()
    adaln_ffn(nc, *args, out)
    r = run_bass_kernel_spmd(nc, [arrays], core_ids=[0])
    got = r.results[0]["out"]
    return np.ascontiguousarray(got.reshape(D, TOK).T).reshape(B, CH, D)
```

```python
import concourse.bass as bass
from concourse import mybir
from contextlib import ExitStack

B, CH, D = 32, 64, 1024
H, DH, M = 16, 64, 256
E_IN, HID, K = 128, 128, 8
P = 128
TOK = B * CH
TW = 512
QT = TOK // TW
CHUNKS = D // P
TILES = CHUNKS * QT
BQ = B // QT
PAIRS = BQ // 2
HEADS = P // DH
MC = M // P
RING = 2 * QT
LAG = 2
OB = CH // 16
ROWS = D * QT

C_EMB = 0
C_W0 = C_EMB + B
C_B0 = C_W0 + HID
C_FIRST = C_B0 + 1
C_W1 = C_FIRST
C_B1 = C_W1 + HID
C_W2 = C_B1 + 1
C_B2 = C_W2 + K
C_ID = C_B2 + K
C_SEL = C_ID + P
C_BK = C_SEL + 16
C_COND = C_BK + CH
C_WK = C_COND
C_ALL = C_WK + OB * CH


def adaln_ffn(nc, xt, perm, packed, up_l, down_l, out):
    f32, f32r, i32 = mybir.dt.float32, mybir.dt.float32r, mybir.dt.int32
    ALU, ACT, AX = mybir.AluOpType, mybir.ActivationFunctionType, mybir.AxisListType

    ctx = ExitStack()
    with ctx:
        def sb(name, shape, dt=f32):
            return ctx.enter_context(nc.sbuf_tensor(name, shape, dt))

        def sem(name):
            return ctx.enter_context(nc.semaphore(name))

        cond = sb("cond", [P, C_ALL])
        h1 = sb("h1", [P, B])
        h2 = sb("h2", [P, B])
        logits = sb("logits", [B, K])
        neg_top = sb("neg_top", [B, 1])
        expd = sb("expd", [B, K])
        warm = sb("warm", [B, 1])
        total = sb("total", [B, 1])
        inv_total = sb("inv_total", [B, 1])
        att_rep = sb("att_rep", [B, K, 16])
        att_sel = sb("att_sel", [P, B, 16])
        att_t = sb("att_t", [P, B])
        mix_b_row = sb("mix_b_row", [B, CH])
        bias_terms = sb("bias_terms", [P, BQ, CH])
        ones = sb("ones", [P, P])
        mix_w = sb("mix_w", [P, B // 2, 2, CH])
        mix_b = sb("mix_b", [P, TOK])
        bias_dram = nc.dram_tensor("bias_dram", (TOK,), f32, kind="Internal").ap()
        perm_sb = sb("perm_sb", [P, CHUNKS], i32)
        idx_all = sb("idx_all", [P, CHUNKS, QT], i32)
        idx = sb("idx", [P, RING], i32)
        g = sb("g", [P, RING, TW])
        xp = sb("xp", [P, 2, TW])
        t = sb("t", [P, 2, TW])
        ts = sb("ts", [P, 2, HEADS, TW], f32r)
        hid = sb("hid", [P, 2, MC, HEADS, TW])
        up_raw = sb("up_raw", [P, 2, HEADS, M])
        up_hi = sb("up_hi", [P, 2, HEADS, M], f32r)
        up_lo = sb("up_lo", [P, 2, HEADS, M], f32r)
        dn = sb("dn", [P, 2, HEADS, MC, DH])

        ps = ctx.enter_context(nc.psum_tensor("ps", [P, 8, TW], f32))
        HB, XB, TB, YB = 0, 4, 5, 6

        s_perm, s_first, s_cond, s_experts = sem("s_perm"), sem("s_first"), sem("s_cond"), sem("s_experts")
        s_idx_all, s_idx, s_passed = sem("s_idx_all"), sem("s_idx"), sem("s_passed")
        s_zero = sem("s_zero")
        s_cmm, s_cact, s_cdve = sem("s_cmm"), sem("s_cact"), sem("s_cdve")
        s_sel = sem("s_sel")
        s_att_t, s_aggb, s_bias_row, s_bias_out = sem("s_att_t"), sem("s_aggb"), sem("s_bias_row"), sem("s_bias_out")
        s_aggw, s_mixw_odd, s_mixw_even, s_mixw_last = sem("s_aggw"), sem("s_mixw_odd"), sem("s_mixw_even"), sem("s_mixw_last")
        s_mixb = [sem(f"s_mixb{q}") for q in range(QT)]
        s_ones, s_terms = sem("s_ones"), sem("s_terms")
        s_gathered = [sem(f"s_gathered{r}") for r in range(RING)]
        s_scattered = [sem(f"s_scattered{r}") for r in range(RING)]
        s_up = [sem(f"s_up{r}") for r in range(2)]
        s_dn = [sem(f"s_dn{r}") for r in range(2)]
        s_up_hi, s_up_split = sem("s_up_hi"), sem("s_up_split")
        s_trans, s_xp = sem("s_trans"), sem("s_xp")
        s_mix, s_t = sem("s_mix"), sem("s_t")
        s_hi, s_lo = sem("s_hi"), sem("s_lo")
        s_upped, s_gelu = sem("s_upped"), sem("s_gelu")
        s_down, s_final = sem("s_down"), sem("s_final")

        def steps(eng, step):
            for r in range(-2, 3):
                step(0, r)
            with eng.Fori(0, TILES - 2 * RING + 1, RING) as base:
                for r in range(3, RING + 3):
                    step(base, r)
            for r in range(3, RING + 1):
                step(TILES - RING, r)

        def exists(base, r):
            return not isinstance(base, int) or 0 <= base + r < TILES

        def first(base, r):
            return r if isinstance(base, int) and base == 0 else None

        PARTS = [(0, PAIRS), (PAIRS, 2 * PAIRS), (2 * PAIRS, B // 2)]
        PART_BANK = [YB + 1, YB, YB + 1]

        def aggregated(part, odd, n=None):
            rows, size = slice(odd * DH, (odd + 1) * DH), (PARTS[part][1] - PARTS[part][0]) * 16
            whole = ps[rows, PART_BANK[part], 0:OB * size].rearrange("p (n a o) -> p n a o", n=OB, o=16)
            return whole if n is None else whole[:, n, :, :]

        def blocks(part, odd):
            return mix_w[odd * DH:(odd + 1) * DH, PARTS[part][0]:PARTS[part][1], odd, :].rearrange(
                "p a (n o) -> p n a o", n=OB)

        block = ctx.enter_context(nc.Block())

        @block.sync
        def _(sp):
            sp.dma_start(cond[:, 0:C_FIRST], packed[:, 0:C_FIRST]).then_inc(s_first, 16)
            sp.dma_start(cond[:, C_FIRST:C_COND], packed[:, C_FIRST:C_COND]).then_inc(s_cond, 16)

            def load(up_row, down_row, r):
                for half in range(2):
                    sp.dma_start(up_raw[half * DH:(half + 1) * DH, r, :, :].rearrange("p e m -> p (e m)"),
                                 up_l[bass.ds(up_row, DH), :]).then_inc(s_up[r], 16)
                sp.dma_start(dn[:, r, :, :, :].rearrange("p e c d -> p (e c d)"),
                             down_l[bass.ds(down_row, P), :]).then_inc(s_dn[r], 16)

            sp.dma_start(cond[:, C_COND:C_ALL], packed[:, C_COND:C_ALL]).then_inc(s_experts, 16)
            load(0, 0, 0)
            sp.wait_ge(s_bias_row, 1)
            sp.dma_start(bias_dram.rearrange("(b o) -> b o", o=CH), mix_b_row[:, :]).then_inc(s_bias_out, 16)
            sp.wait_ge(s_bias_out, 16)
            for q in list(range(1, QT)) + [0]:
                sp.dma_start(mix_b[:, q * TW:(q + 1) * TW],
                             bias_dram[q * TW:(q + 1) * TW].rearrange("(a n) -> a n", a=1).broadcast_to((P, TW))
                             ).then_inc(s_mixb[q], 16)
            load(DH, P, 1)
            with sp.Fori(2, CHUNKS - 1, 2) as chunk:
                for r in range(2):
                    sp.wait_ge(s_down, (chunk + (r - 1)) * QT)
                    load((chunk + r) * DH, (chunk + r) * P, r)

        @block.gpsimd
        def _(pool):
            nc.gpsimd.memset(ones[:, :], 1.0).then_inc(s_ones, 1)
            nc.gpsimd.memset(mix_w[:, :, :, :], 0.0).then_inc(s_zero, 1)

            def gather(r, rows):
                pool.indirect_dma_start(out=g[:, r, :], out_offset=None, in_=xt,
                                        in_offset=bass.IndirectOffsetOnAxis(ap=rows, axis=0),
                                        ).then_inc(s_gathered[r], 16)

            def split(base, c):
                r = c % 2
                pool.wait_ge(s_up[r], (base + c - r) * 16 + 32)
                if not isinstance(base, int) or base + c >= 2:
                    pool.wait_ge(s_upped, (base + (c - 1)) * QT * MC)
                    pool.sem_inc(s_passed, 1)
                nc.gpsimd.tensor_copy(up_hi[:, r, :, :], up_raw[:, r, :, :]).then_inc(s_up_hi, 1)
                pool.wait_ge(s_up_hi, base + c + 1)
                nc.gpsimd.tensor_tensor(up_lo[:, r, :, :], up_raw[:, r, :, :], up_hi[:, r, :, :].bitcast(f32),
                                        ALU.subtract).then_inc(s_up_split, 1)

            for r in range(RING):
                if r < QT:
                    pool.wait_ge(s_idx_all, r + 1)
                gather(r, idx_all[:, r // QT, r % QT:r % QT + 1])
                if r == 3:
                    split(0, 0)
            split(0, 1)
            nc.gpsimd.tensor_copy(idx[:, :], idx_all[:, 0:2, :].rearrange("p c q -> p (c q)")).then_inc(s_idx, 1)
            pool.wait_ge(s_idx, 1)

            def scatter(base, r):
                slot = r % RING
                pool.wait_ge(s_final, base + r + 1)
                pool.sem_inc(s_passed, 1)
                pool.indirect_dma_start(out=out,
                                        out_offset=bass.IndirectOffsetOnAxis(ap=idx[:, slot:slot + 1], axis=0),
                                        in_=g[:, slot, :], in_offset=None).then_inc(s_scattered[slot], 16)

            def refill(base, r):
                pool.wait_ge(s_scattered[r], base * (16 // RING) + 16)
                nc.gpsimd.tensor_copy(idx[:, r:r + 1], idx_flat[:, bass.ds(base + (RING + r), 1)]).then_inc(s_idx, 1)
                pool.wait_ge(s_idx, base + (r + 2))
                pool.sem_inc(s_passed, 1)
                gather(r, idx[:, r:r + 1])

            idx_flat = idx_all[:, :, :].rearrange("p c q -> p (c q)")
            for r in range(LAG):
                scatter(0, r)
            with pool.Fori(0, TILES - 2 * RING + 1, RING) as base:
                for r in range(RING):
                    scatter(base, r + LAG)
                    refill(base, r)
                    if r % QT == 2:
                        split(base // QT, 2 + r // QT)
            for r in range(LAG, RING):
                scatter(TILES - RING, r)
            for r in range(RING):
                pool.wait_ge(s_scattered[r], (TILES // RING) * 16)

        @block.scalar
        def _(act):
            b0, b1 = cond[:, C_B0:C_B0 + 1], cond[:, C_B1:C_B1 + 1]
            act.dma_start(perm_sb[:, :], perm).then_inc(s_perm, 16)
            act.wait_ge(s_cmm, 1)
            nc.scalar.activation(h1[:, :], ps[:, HB, 0:B], ACT.Gelu, bias=b0).then_inc(s_cact, 1)
            act.wait_ge(s_cmm, 2)
            nc.scalar.activation(h2[:, :], ps[:, HB, 64:64 + B], ACT.Gelu, bias=b1).then_inc(s_cact, 1)
            act.wait_ge(s_cdve, 2)
            nc.scalar.activation(expd[:, :], logits[:, :], ACT.Exp, bias=neg_top[:, :],
                                 accum_out=total[:, :]).then_inc(s_cact, 1)
            nc.scalar.activation(warm[:, :], neg_top[:, :], ACT.Gelu)

            act.wait_ge(s_aggb, 1)
            nc.scalar.activation(mix_b_row[:, :], ps[0:B, YB, 0:CH], ACT.Copy).then_inc(s_bias_row, 1)

            def take_mix(part):
                if part == 0:
                    act.wait_ge(s_zero, 1)
                act.wait_ge(s_aggw, part + 1)
                nc.scalar.activation(blocks(part, 1), aggregated(part, 1), ACT.Copy).then_inc(s_mixw_odd, 1)
                if part == 2:
                    nc.scalar.activation(blocks(2, 0), aggregated(2, 0), ACT.Copy).then_inc(s_mixw_last, 1)

            def hi(base, r, e):
                if not exists(base, r):
                    return
                act.wait_ge(s_t, base + r + 1)
                if not isinstance(base, int) or base + r >= 2:
                    act.wait_ge(s_upped, (base + (r - 1)) * MC)
                rows = slice(e * DH, (e + 1) * DH)
                nc.scalar.activation(ts[rows, r % 2, e, :], t[rows, r % 2, :], ACT.Copy).then_inc(s_hi, 1)

            def gelu(base, r, c):
                if not exists(base, r):
                    return
                act.wait_ge(s_upped, (base + r) * MC + c + 1)
                if not isinstance(base, int) or base + r >= 2:
                    act.wait_ge(s_down, (base + (r - 1)))
                nc.scalar.activation(hid[:, r % 2, c, :, :], ps[:, HB + 2 * c:HB + 2 * c + 2, :],
                                     ACT.Gelu).then_inc(s_gelu, 1)

            def step(base, r):
                if first(base, r) == -1:
                    take_mix(0)
                    take_mix(1)
                hi(base, r + 1, 0)
                hi(base, r + 1, 1)
                if first(base, r) == -1:
                    take_mix(2)
                gelu(base, r, 0)
                gelu(base, r, 1)

            steps(act, step)

        @block.vector
        def _(dve):
            dve.wait_ge(s_perm, 16)
            for q in range(QT):
                nc.vector.tensor_scalar(idx_all[:, :, q], perm_sb[:, :], QT, q, ALU.mult, ALU.add).then_inc(s_idx_all, 1)
            dve.wait_ge(s_cmm, 3)
            nc.vector.tensor_tensor(logits[:, :], ps[0:B, HB, 128:128 + K], cond[0:B, C_B2:C_B2 + K],
                                    ALU.add).then_inc(s_cdve, 1)
            dve.wait_ge(s_cdve, 1)
            nc.vector.tensor_reduce(neg_top[:, :], logits[:, :], AX.X, ALU.max, negate=True).then_inc(s_cdve, 1)
            dve.wait_ge(s_cact, 3)
            nc.vector.reciprocal(inv_total[:, :], total[:, :]).then_inc(s_cdve, 1)
            dve.wait_ge(s_cdve, 3)
            nc.vector.tensor_scalar(att_rep[:, :, :], expd[:, :].rearrange("p (k a) -> p k a", a=1).broadcast_to((B, K, 16)),
                                    inv_total[:, :], None, ALU.mult).then_inc(s_cdve, 1)
            dve.wait_ge(s_cmm, 4)

            def expert_biases():
                dve.wait_ge(s_att_t, 1)
                nc.vector.tensor_tensor(bias_terms[:, :, :],
                                        att_t[:, 0:BQ].rearrange("p (b a) -> p b a", a=1).broadcast_to((P, BQ, CH)),
                                        cond[:, C_BK:C_BK + CH].rearrange("p (a o) -> p a o", a=1).broadcast_to((P, BQ, CH)),
                                        ALU.mult).then_inc(s_terms, 1)

            def select(q):
                nc.vector.tensor_tensor(att_sel[:, q * BQ:(q + 1) * BQ, :],
                                        ps[:, HB, 192 + q * BQ:192 + (q + 1) * BQ].rearrange("p (b a) -> p b a", a=1).broadcast_to((P, BQ, 16)),
                                        cond[:, C_SEL:C_SEL + 16].rearrange("p (a o) -> p a o", a=1).broadcast_to((P, BQ, 16)),
                                        ALU.mult).then_inc(s_sel, 1)

            def take_mix(part):
                if part == 0:
                    dve.wait_ge(s_zero, 1)
                dve.wait_ge(s_aggw, part + 1)
                nc.vector.tensor_copy(blocks(part, 0), aggregated(part, 0)).then_inc(s_mixw_even, 1)

            def take_xp(base, r):
                if not exists(base, r):
                    return
                dve.wait_ge(s_trans, base + r + 1)
                if not isinstance(base, int) or base + r >= 2:
                    dve.wait_ge(s_mix, base + (r - 1))
                nc.vector.tensor_copy(xp[:, r % 2, :], ps[:, XB, :]).then_inc(s_xp, 1)

            def take_t(base, r):
                if not exists(base, r):
                    return
                q = r % QT
                if isinstance(base, int) and 1 <= base + r < QT:
                    dve.wait_ge(s_mixb[r], 16)
                    if r == QT - 1:
                        dve.wait_ge(s_mixb[0], 16)
                dve.wait_ge(s_mix, base + r + 1)
                if not isinstance(base, int) or base + r >= 2:
                    dve.wait_ge(s_hi, (base + (r - 1)) * HEADS)
                if first(base, r) == 0:
                    nc.vector.tensor_copy(t[:, 0, :], ps[:, TB, :]).then_inc(s_t, 1)
                    return
                nc.vector.tensor_tensor(t[:, r % 2, :], ps[:, TB, :],
                                        mix_b[:, q * TW:(q + 1) * TW],
                                        ALU.add).then_inc(s_t, 1)

            def lo(base, r, e):
                if not exists(base, r):
                    return
                dve.wait_ge(s_hi, (base + r) * HEADS + e + 1)
                rows = slice(e * DH, (e + 1) * DH)
                other = slice((1 - e) * DH, (2 - e) * DH)
                nc.vector.tensor_tensor(ts[other, r % 2, e, :], t[rows, r % 2, :], ts[rows, r % 2, e, :].bitcast(f32),
                                        ALU.subtract).then_inc(s_lo, 1)

            def final(base, r):
                if not exists(base, r):
                    return
                dve.wait_ge(s_down, base + r + 1)
                nc.vector.tensor_tensor(g[:, r % RING, :], ps[:, YB + r % 2, :], g[:, r % RING, :],
                                        ALU.add).then_inc(s_final, 1)

            nc.vector.tensor_copy(att_t[:, :], ps[:, HB, 192:192 + B]).then_inc(s_att_t, 1)
            select(0)
            expert_biases()

            def step(base, r):
                if first(base, r) == -1:
                    take_mix(0)
                    for q in range(1, QT):
                        select(q)
                take_t(base, r + 1)
                if first(base, r) == -1:
                    take_mix(1)
                take_xp(base, r + 2)
                lo(base, r + 1, 0)
                lo(base, r + 1, 1)
                final(base, r - 1)

            steps(dve, step)

        @block.tensor
        def _(pe):
            ident = cond[:, C_ID:C_ID + P]
            pe.wait_ge(s_first, 16)

            def warm_up(n):
                for _ in range(n):
                    nc.tensor.matmul(ps[:, YB + 1, 0:HID], cond[:, C_W0:C_W0 + HID], cond[:, C_W0:C_W0 + HID],
                                     start=True, stop=True)

            nc.tensor.matmul(ps[:, HB, 0:B], cond[:, C_W0:C_W0 + HID], cond[:, C_EMB:C_EMB + B],
                             start=True, stop=True).then_inc(s_cmm, 1)
            warm_up(2)
            pe.wait_ge(s_cond, 16)
            pe.wait_ge(s_cact, 1)
            nc.tensor.matmul(ps[:, HB, 64:64 + B], cond[:, C_W1:C_W1 + HID], h1[:, :],
                             start=True, stop=True).then_inc(s_cmm, 1)
            warm_up(1)
            pe.wait_ge(s_cact, 2)
            nc.tensor.matmul(ps[0:B, HB, 128:128 + K], h2[:, :], cond[:, C_W2:C_W2 + K],
                             start=True, stop=True).then_inc(s_cmm, 1)

            def aggregate(part):
                if part == 0:
                    pe.wait_ge(s_experts, 16)
                elif part == 1:
                    pe.wait_ge(s_bias_row, 1)
                pe.wait_ge(s_sel, (1, 2, QT)[part])
                for odd in range(2):
                    for n in range(OB):
                        last = nc.tensor.matmul(
                            aggregated(part, odd, n), cond[:, C_WK + n * CH:C_WK + (n + 1) * CH],
                            att_sel[:, :, :].rearrange("p (a h) o -> p a h o", h=2)[:, PARTS[part][0]:PARTS[part][1], odd, :],
                            start=True, stop=True)
                last.then_inc(s_aggw, 1)

            def trans(base, r):
                if not exists(base, r):
                    return
                slot = r % RING
                pe.wait_ge(s_gathered[slot], (base + (r - slot)) * (16 // RING) + 16)
                if not isinstance(base, int) or base + r >= 1:
                    pe.wait_ge(s_xp, base + r)
                for a in range(PAIRS):
                    last = nc.tensor.transpose(ps[:, XB, a * P:(a + 1) * P], g[:, slot, a * P:(a + 1) * P], ident)
                last.then_inc(s_trans, 1)

            warm_up(3)
            pe.wait_ge(s_cdve, 4)
            nc.tensor.matmul(ps[:, HB, 192:192 + B], att_rep[:, :, :].rearrange("p k a -> p (k a)"),
                             cond[0:B, C_ID:C_ID + B], start=True, stop=True).then_inc(s_cmm, 1)
            trans(0, 0)
            pe.wait_ge(s_att_t, 1)
            nc.tensor.matmul(ps[0:B, YB, 0:CH], att_t[:, :], cond[:, C_BK:C_BK + CH],
                             start=True, stop=True).then_inc(s_aggb, 1)

            def mix(base, r):
                if not exists(base, r):
                    return
                early = first(base, r) == 0
                if early:
                    pe.wait_ge(s_ones, 1)
                    pe.wait_ge(s_terms, 1)
                    nc.tensor.matmul(ps[:, TB, :], ones[:, :], bias_terms[:, :, :].rearrange("p b o -> p (b o)"),
                                     start=True, stop=False)
                pe.wait_ge(s_xp, base + r + 1)
                if isinstance(base, int) and base + r <= 2:
                    pe.wait_ge(s_mixw_odd, r + 1)
                    if r < 2:
                        pe.wait_ge(s_mixw_even, r + 1)
                    else:
                        pe.wait_ge(s_mixw_last, 1)
                if not isinstance(base, int) or base + r >= 1:
                    pe.wait_ge(s_t, base + r)
                for a in range(PAIRS):
                    pair = (r % QT) * PAIRS + a
                    last = nc.tensor.matmul(ps[:, TB, a * P:(a + 1) * P], xp[:, r % 2, a * P:(a + 1) * P],
                                            mix_w[:, pair, :, :].rearrange("p h o -> p (h o)"),
                                            start=not early, stop=not early or a == PAIRS - 1)
                last.then_inc(s_mix, 1)

            def up(base, r, c):
                if not exists(base, r):
                    return
                w = (r % RING) // QT
                if c == 0:
                    if r % QT == 0:
                        pe.wait_ge(s_up_split, (base // QT) + (r // QT + 1))
                if not isinstance(base, int) or base + r >= 1:
                    pe.wait_ge(s_gelu, (base + (r - 1)) * MC + c + 1)
                for e in range(HEADS):
                    if c == 0:
                        pe.wait_ge(s_lo, (base + r) * HEADS + (e + 1))
                    for n, wt in enumerate((up_hi, up_lo)):
                        last = nc.tensor.matmul(ps[:, HB + 2 * c + e, :], wt[:, w, e, c * P:(c + 1) * P],
                                                ts[:, r % 2, e, :], start=(n == 0), stop=(n == 1))
                last.then_inc(s_upped, 1)

            def down(base, r, c):
                if not exists(base, r):
                    return
                slot = r % RING
                w = slot // QT
                if c == 0:
                    if r % QT == 0:
                        pe.wait_ge(s_dn[w], (base + (r - slot)) * (16 // RING) + 16)
                    if not isinstance(base, int) or base + r >= 2:
                        pe.wait_ge(s_final, base + (r - 1))
                pe.wait_ge(s_gelu, (base + r) * MC + c + 1)
                for e in range(HEADS):
                    last = nc.tensor.matmul(ps[e * DH:(e + 1) * DH, YB + r % 2, :], dn[:, w, e, c, :],
                                            hid[:, r % 2, c, e, :], start=(c == 0), stop=(c == MC - 1))
                if c == MC - 1:
                    last.then_inc(s_down, 1)

            def step(base, r):
                if first(base, r) == -1:
                    aggregate(0)
                mix(base, r + 1)
                if first(base, r) == -1:
                    aggregate(1)
                if first(base, r) != -2:
                    trans(base, r + 2)
                up(base, r, 0)
                up(base, r, 1)
                if first(base, r) == -1:
                    aggregate(2)
                down(base, r - 1, 0)
                down(base, r - 1, 1)

            steps(pe, step)


def kernel(**inputs):
    import numpy as np
    import concourse.bacc as bacc
    from concourse import mybir as mb
    from concourse.bass_utils import run_bass_kernel_spmd

    a = {name: np.asarray(v) for name, v in inputs.items()}
    xt = np.ascontiguousarray(a["x"].reshape(TOK, D).T).reshape(ROWS, TW)
    perm = np.ascontiguousarray(a["L0_ffn_perm"].reshape(CHUNKS, P).T)
    bcast = lambda v: np.broadcast_to(v, (P,) + v.shape)
    experts = a["L0_cond_weight"].reshape(K, OB, 16, CH).transpose(0, 2, 1, 3).reshape(P, OB * CH)
    bias_k = np.zeros((K, 16, CH), np.float32)
    bias_k[:, 0] = a["L0_cond_bias_k"]
    packed = np.concatenate([
        a["cond_128"].T, a["L0_cond_W0"], a["L0_cond_b0"].reshape(P, 1),
        a["L0_cond_W1"], a["L0_cond_b1"].reshape(P, 1), a["L0_cond_W2"], bcast(a["L0_cond_b2"]),
        np.eye(P, dtype=np.float32), np.tile(np.eye(16, dtype=np.float32), (K, 1)),
        bias_k.reshape(P, CH), experts,
    ], axis=1)
    up_l = np.ascontiguousarray(a["L0_ffn_up"].reshape(CHUNKS, HEADS, DH, M).transpose(0, 2, 1, 3)).reshape(CHUNKS * DH, HEADS * M)
    down_l = np.ascontiguousarray(a["L0_ffn_down"].reshape(CHUNKS, HEADS, MC, P, DH).transpose(0, 3, 1, 2, 4)).reshape(CHUNKS * P, HEADS * MC * DH)

    nc = bacc.Bacc("TRN2", target_bir_lowering=False, num_devices=1)
    arrays, args = {}, []
    for name, v in (("xt", xt), ("perm", perm), ("packed", packed), ("up_l", up_l), ("down_l", down_l)):
        arrays[name] = v
        args.append(nc.dram_tensor(name, v.shape, mb.dt.from_np(v.dtype), kind="ExternalInput").ap())
    out = nc.dram_tensor("out", (ROWS, TW), mb.dt.float32, kind="ExternalOutput").ap()
    adaln_ffn(nc, *args, out)
    r = run_bass_kernel_spmd(nc, [arrays], core_ids=[0])
    got = r.results[0]["out"]
    return np.ascontiguousarray(got.reshape(D, TOK).T).reshape(B, CH, D)
```
